# Optimizing a Trainium2 kernel written in Bass

```python
import numpy as np
import jax
import jax.numpy as jnp

def _softmax(x, axis=-1):
    return jax.nn.softmax(x, axis=axis)

def _gelu(x):
    return jax.nn.gelu(x, approximate=True)

def _silu(x):
    return jax.nn.silu(x)

def _sigmoid(x):
    return jax.nn.sigmoid(x)

def _layernorm(x, axis=-1, eps=1e-05):
    m = jnp.mean(x, axis=axis, keepdims=True)
    v = jnp.var(x, axis=axis, keepdims=True)
    return (x - m) / jnp.sqrt(v + eps)

def _scatter_add(tgt, idx, src, axis=0):
    return tgt.at[idx].add(src)

def _segment_sum(src, seg, n):
    return jax.ops.segment_sum(src, seg, n)
kernel_name = 'mk_gnn_preln_d2_gnn_r32_c5fe02'

def setup_inputs(seed: int=0):
    np.random.seed(seed)
    _w = jnp.asarray

    def _rec_inputs():
        import jax
        import jax.numpy as jnp
        _gk = jax.random.key(seed)
        x = -0.0003713 + 1 * jax.random.normal(jax.random.fold_in(_gk, 1), (3125, 128), jnp.float32)
        src = jax.random.randint(jax.random.fold_in(_gk, 2), (50000,), 0, 3125, jnp.int32)
        dst = jnp.minimum((3125 * jax.random.uniform(jax.random.fold_in(_gk, 3), (50000,)) ** 2.0).astype(jnp.int32), 99999)
        _o = jnp.argsort(dst, stable=True)
        src = src[_o]
        dst = dst[_o]
        return (x, src, dst)
    x, src, dst = _rec_inputs()

    def _L0_gnn_setup():
        import jax, jax.numpy as jnp
        import numpy as np
        N_NODES = 3125
        N_EDGES = 20000
        IN_FEATS = 128
        OUT_FEATS = 128
        key = jax.random.key(seed)
        k1, k2, k3, k4, k5 = jax.random.split(key, 5)
        feature = jax.random.normal(k1, (N_NODES, IN_FEATS), dtype=jnp.float32)
        src = jax.random.randint(k2, (N_EDGES,), 0, N_NODES, dtype=jnp.int64)
        dst = jax.random.randint(k3, (N_EDGES,), 0, N_NODES, dtype=jnp.int64)
        bound = 1.0 / np.sqrt(IN_FEATS)
        W = jax.random.uniform(k4, (OUT_FEATS, IN_FEATS), minval=-bound, maxval=bound, dtype=jnp.float32)
        b = jax.random.uniform(k5, (OUT_FEATS,), minval=-bound, maxval=bound, dtype=jnp.float32)
        return {'feature': feature, 'src': src, 'dst': dst, 'W': W, 'b': b}
    _L0_gnn_all = _L0_gnn_setup()
    _L0_gnn_in = {k: v for k, v in _L0_gnn_all.items() if k in ('W', 'b')}
    del _L0_gnn_all

    def _L1_gnn_setup():
        import jax, jax.numpy as jnp
        import numpy as np
        N_NODES = 50000
        N_EDGES = 25000
        IN_DIM = 128
        HID = 128
        TIME = 6.0
        STEPS = 12
        key = jax.random.key(seed)
        ks = jax.random.split(key, 8)
        gat_out = jax.random.normal(ks[0], (N_NODES, IN_DIM), dtype=jnp.float32)
        edge_index = jax.random.randint(ks[1], (2, N_EDGES), 0, N_NODES, dtype=jnp.int64)
        W_in = jax.random.normal(ks[2], (IN_DIM, HID), dtype=jnp.float32) * (1.0 / np.sqrt(IN_DIM))
        b_in = jnp.zeros((HID,), dtype=jnp.float32)
        W1 = jax.random.normal(ks[3], (HID, 2 * HID), dtype=jnp.float32) * (1.0 / np.sqrt(HID))
        b1 = jnp.zeros((2 * HID,), dtype=jnp.float32)
        W2 = jax.random.normal(ks[4], (2 * HID, HID), dtype=jnp.float32) * (1.0 / np.sqrt(2 * HID))
        b2 = jnp.zeros((HID,), dtype=jnp.float32)
        clearance = jnp.full((1,), 0.1, dtype=jnp.float32)
        return {'gat_out': gat_out, 'edge_index': edge_index, 'W_in': W_in, 'b_in': b_in, 'W1': W1, 'b1': b1, 'W2': W2, 'b2': b2, 'clearance': clearance}
    _L1_gnn_all = _L1_gnn_setup()
    _L1_gnn_in = {k: v for k, v in _L1_gnn_all.items() if k in ('W_in', 'b_in', 'W1', 'b1', 'W2', 'b2', 'clearance')}
    del _L1_gnn_all
    return {'x': x, 'src': src, 'dst': dst, 'L0_gnn_W': _L0_gnn_in['W'], 'L0_gnn_b': _L0_gnn_in['b'], 'L1_gnn_W_in': _L1_gnn_in['W_in'], 'L1_gnn_b_in': _L1_gnn_in['b_in'], 'L1_gnn_W1': _L1_gnn_in['W1'], 'L1_gnn_b1': _L1_gnn_in['b1'], 'L1_gnn_W2': _L1_gnn_in['W2'], 'L1_gnn_b2': _L1_gnn_in['b2'], 'L1_gnn_clearance': _L1_gnn_in['clearance']}

def reference(x, src, dst, L0_gnn_W, L0_gnn_b, L1_gnn_W_in, L1_gnn_b_in, L1_gnn_W1, L1_gnn_b1, L1_gnn_W2, L1_gnn_b2, L1_gnn_clearance):
    import jax
    import jax.numpy as jnp

    def _L0_gnn_ref(feature, src, dst, W, b):
        import jax, jax.numpy as jnp
        import numpy as np
        N_NODES = 3125
        N_EDGES = 20000
        IN_FEATS = 128
        OUT_FEATS = 128
        msgs = feature[src]
        h = jax.ops.segment_sum(msgs, dst, num_segments=N_NODES)
        return h @ W.T + b

    def _L1_gnn_ref(gat_out, edge_index, W_in, b_in, W1, b1, W2, b2, clearance):
        import jax, jax.numpy as jnp
        import numpy as np
        N_NODES = 50000
        N_EDGES = 25000
        IN_DIM = 128
        HID = 128
        TIME = 6.0
        STEPS = 12
        N = gat_out.shape[0]
        dt = TIME / STEPS
        src, dst = (edge_index[0], edge_index[1])
        h = jnp.tanh(gat_out @ W_in + b_in)
        deg = jax.ops.segment_sum(jnp.ones((src.shape[0],), dtype=h.dtype), dst, num_segments=N)
        deg = jnp.clip(deg, 1.0, None)[:, None]
        decay = jax.nn.relu(clearance)

        def step(h, _):
            agg = jax.ops.segment_sum(h[src], dst, num_segments=N) / deg
            diff = jnp.tanh(jax.nn.gelu(agg @ W1 + b1, approximate=False) @ W2 + b2)
            h = h + (diff - decay * h) * dt
            return (h, None)
        h, _ = jax.lax.scan(step, h, None, length=STEPS)
        return h
    edge_index = jnp.stack([src, dst])
    h = jnp.maximum(_layernorm(x, axis=-1), 0.0)
    x = x + _L0_gnn_ref(h, src, dst, L0_gnn_W, L0_gnn_b)
    h = jnp.maximum(_layernorm(x, axis=-1), 0.0)
    x = x + _L1_gnn_ref(h, edge_index, L1_gnn_W_in, L1_gnn_b_in, L1_gnn_W1, L1_gnn_b1, L1_gnn_W2, L1_gnn_b2, L1_gnn_clearance)
    return x

_drawn_inputs = setup_inputs


def setup_inputs(seed=0):
    import zlib

    import numpy as np

    out = dict(_drawn_inputs(seed))
    spreads = {'L1_gnn_b_in': (0.0, 0.1), 'L1_gnn_b1': (0.0, 0.1), 'L1_gnn_b2': (0.0, 0.1)}
    factors = {'L0_gnn_b': 6.317}
    for name, (base, spread) in spreads.items():
        noise = np.random.default_rng([zlib.crc32(name.encode()), seed]).standard_normal(out[name].shape)
        drawn = base * np.exp(spread * noise) if base else spread * noise
        out[name] = jnp.asarray(drawn.astype(out[name].dtype))
    for name, factor in factors.items():
        out[name] = (out[name] * factor).astype(out[name].dtype)
    return out
```

```python
from contextlib import ExitStack

import concourse.bass as bass
from concourse import mybir

ALU = mybir.AluOpType
ACT = mybir.ActivationFunctionType
AX = mybir.AxisListType
F32 = mybir.dt.float32
F16 = mybir.dt.float16
I32 = mybir.dt.int32

P = 128
STEPS = 12
DT = 6.0 / STEPS
EPS = 1e-5
LN_SCALE = 2.0 ** 11
CH = 512
ds = bass.ds


def wait(eng, sem, value):
    if not (isinstance(value, int) and value <= 0):
        eng.wait_ge(sem, value)


class Chain:

    def __init__(self, eng, sem, base=0):
        self.eng, self.sem, self.base, self.n = eng, sem, base, 0

    def __call__(self, ins):
        ins.then_inc(self.sem, 1)
        self.n += 1
        self.eng.wait_ge(self.sem, self.base + self.n)


def graph_layers_kernel(nc, x, src, dst, W0, b0, W_in, b_in, W1, b1, W2, b2, clearance, out):
    N, D = x.shape
    E = src.shape[0]
    HID = W1.shape[1]
    KT = -(-N // P)
    LASTK = N - (KT - 1) * P
    NF = N // CH
    TAIL = N - NF * CH
    TPC = CH // P
    EC = -(-E // P)
    ELAST = E - (P - 1) * EC
    NCH = NF + 1
    PW = KT * 2 * D
    assert D == P and HID == 2 * D and NF * TPC == KT - 1 and 0 < ELAST <= EC and TAIL == LASTK

    rdeg_dram = nc.dram_tensor("rdeg_scratch", [NCH, P, CH], F32, kind="Internal").ap()
    x1_dram = nc.dram_tensor("x1_scratch", [N, D], F32, kind="Internal").ap()

    def node_rows(dram, j):
        if isinstance(j, int) and j == NF:
            return dram[NF * CH:N, :]
        return dram[ds(j * CH, CH), :].rearrange("(a p) d -> p a d", p=P)

    with ExitStack() as ctx:
        def sb(name, shape, dt=F32):
            return ctx.enter_context(nc.sbuf_tensor(name, shape, dt))

        def sem(name):
            return ctx.enter_context(nc.semaphore(name))

        adj = sb("adj", [P, KT * N], F16)
        parts = sb("parts", [P, 2 * PW], F16)
        state = sb("state", [P, KT * P])
        rdeg = sb("rdeg", [P, CH])
        rdeg_tail = sb("rdeg_tail", [P, TAIL])
        agg = sb("agg", [P, CH])
        agg_tail = sb("agg_tail", [P, TAIL])
        hidden = sb("hidden", [P, 2, CH])
        scratch = sb("scratch", [P, CH])
        diff = sb("diff", [P, CH])
        w1 = sb("w1", [P, HID])
        w2 = sb("w2", [P, 2, D])
        w_in = sb("w_in", [P, D])
        w0t = sb("w0t", [P, D])
        b0_row = sb("b0_row", [P, D])
        ident = sb("ident", [P, P])
        b1_col = sb("b1_col", [P, 2])
        b2_col = sb("b2_col", [P, 1])
        b_in_col = sb("b_in_col", [P, 1])
        decay = sb("decay", [P, 2])
        bound = sb("bound", [P, STEPS + 1])
        scale = sb("scale", [P, STEPS + 1])
        unscale = sb("unscale", [P, STEPS + 1])
        step_scale = sb("step_scale", [P, 2])
        stat = sb("stat", [P, 8, TPC])

        NPAD = N + N % 2
        onehot_dst = parts[:, 0:2 * NPAD]
        iota_dst = parts[:, 2 * NPAD:2 * NPAD + N]
        src_f = state[:, 0:EC]
        dst_f = state[:, EC:2 * EC]
        src_i = state[:, 2 * EC:3 * EC].bitcast(I32)
        dst_i = state[:, 3 * EC:4 * EC].bitcast(I32)
        onehot_src = state[:, 4 * EC:4 * EC + 128].bitcast(F16)
        iota_src = state[:, 4 * EC + 128:4 * EC + 192].bitcast(F16)

        ps = [ctx.enter_context(nc.psum_tensor(f"bank{i}", [P, CH], F32)) for i in range(8)]

        s_edges, s_w = sem("s_edges"), sem("s_w")
        s_fill, s_iota, s_const = sem("s_fill"), sem("s_iota"), sem("s_const")
        s_edge_f, s_cd = sem("s_edge_f"), sem("s_cd")
        s_w0t, s_id = sem("s_w0t"), sem("s_id")
        with nc.Block() as block:
            @block.sync
            def _(sp):
                sp.wait_ge(s_fill, 2)
                for dram, tile in ((src, src_i), (dst, dst_i)):
                    sp.dma_start(tile[0:P - 1, :], dram[0:(P - 1) * EC].rearrange("(p c) -> p c", c=EC)).then_inc(s_edges, 16)
                    sp.dma_start(tile[P - 1:P, 0:ELAST], dram[(P - 1) * EC:E].rearrange("(p c) -> p c", p=1)).then_inc(s_edges, 16)
                sp.dma_start(agg[:, 0:D], W0).then_inc(s_w, 16)
                sp.dma_start(w_in[:, :], W_in).then_inc(s_w, 16)
                sp.dma_start(w1[:, :], W1).then_inc(s_w, 16)
                sp.dma_start(w2[:, :, :], W2.rearrange("(h p) n -> p h n", p=P)).then_inc(s_w, 16)
                sp.dma_start(b0_row[:, :], b0.rearrange("(a n) -> a n", a=1).broadcast_to([P, D])).then_inc(s_w, 16)
                with nc.allow_non_contiguous_dma("bias columns"):
                    sp.dma_start(b1_col[:, :], b1.rearrange("(h p) -> p h", p=P)).then_inc(s_w, 16)
                    sp.dma_start(b2_col[:, :], b2.rearrange("(p a) -> p a", a=1)).then_inc(s_w, 16)
                    sp.dma_start(b_in_col[:, :], b_in.rearrange("(p a) -> p a", a=1)).then_inc(s_w, 16)
                    sp.dma_start(decay[:, 0:1], clearance.rearrange("(a n) -> a n", a=1).broadcast_to([P, 1])).then_inc(s_w, 16)

            @block.gpsimd
            def _(pool):
                pool.memset(src_i, -1).then_inc(s_fill, 1)
                pool.memset(dst_i, -1).then_inc(s_fill, 1)
                pool.iota(iota_dst, [[1, N]], base=-(N // 2), channel_multiplier=0,
                          allow_small_or_imprecise_dtypes=True).then_inc(s_iota, 1)
                pool.iota(iota_src, [[1, P]], base=0, channel_multiplier=0,
                          allow_small_or_imprecise_dtypes=True).then_inc(s_iota, 1)
                pool.memset(ident[:, :], 0.0).then_inc(s_id, 1)
                pool.wait_ge(s_id, 1)
                pool.affine_select(out=ident[:, :], in_=ident[:, :], compare_op=ALU.not_equal, fill=1.0, base=0,
                                   pattern=[[-1, P]], channel_multiplier=1).then_inc(s_const, 1)

            @block.vector
            def _(dve):
                link = Chain(dve, s_cd)
                dve.wait_ge(s_edges, 64)
                nc.vector.tensor_copy(src_f, src_i)
                nc.vector.tensor_copy(dst_f, dst_i).then_inc(s_edge_f, 1)
                dve.wait_ge(s_edge_f, 1)
                nc.vector.tensor_scalar(dst_f, dst_f, float(-(N // 2)), None, ALU.add).then_inc(s_edge_f, 1)
                dve.wait_ge(s_w, 9 * 16)
                link(nc.vector.tensor_scalar(decay[:, 1:2], decay[:, 0:1], 0.0, -1.0, ALU.max, ALU.mult))
                link(nc.vector.tensor_scalar(stat[:, 0, 0:1], decay[:, 1:2], DT, 1.0, ALU.mult, ALU.add))
                link(nc.vector.tensor_scalar(stat[:, 0, 1:2], stat[:, 0, 0:1], -1.0, None, ALU.mult))
                link(nc.vector.tensor_tensor(stat[:, 0, 0:1], stat[:, 0, 0:1], stat[:, 0, 1:2], ALU.max))
                link(nc.vector.memset(bound[:, 0:1], 1.0))
                for t in range(STEPS):
                    link(nc.vector.tensor_scalar(bound[:, t + 1:t + 2], bound[:, t:t + 1], stat[:, 0, 0:1], DT,
                                                 ALU.mult, ALU.add))
                link(nc.vector.tensor_scalar(unscale[:, :].bitcast(I32), bound[:, :].bitcast(I32), 0x7F800000, None,
                                             ALU.bitwise_and))
                link(nc.vector.tensor_scalar(unscale[:, :], unscale[:, :], 2.0 ** -14, None, ALU.mult))
                link(nc.vector.reciprocal(scale[:, :], unscale[:, :]))
                dve.wait_ge(s_w0t, 1)
                nc.vector.tensor_copy(w0t[:, :], ps[0][:, 0:D])

            @block.tensor
            def _(pe):
                pe.wait_ge(s_w, 9 * 16)
                pe.wait_ge(s_const, 1)
                nc.tensor.transpose(ps[0][:, 0:D], agg[:, 0:D], ident[:, :]).then_inc(s_w0t, 1)

        s_oh, s_ohused, s_full, s_evac, s_rel = (sem("s_oh"), sem("s_ohused"), sem("s_full"), sem("s_evac"),
                                                 sem("s_rel"))
        BPE = 7
        with nc.Block() as block:
            @block.vector
            def _(dve):
                dve.sem_inc(s_evac, 1)
                with dve.Fori(0, KT) as k:
                    with dve.Fori(0, EC) as c:
                        n = k * EC + c
                        dve.wait_ge(s_ohused, n + 1)
                        nc.vector.tensor_scalar(onehot_dst[:, ds((n % 2) * NPAD, N)], iota_dst,
                                                dst_f[:, ds(c, 1)], None, ALU.is_equal)
                        nc.vector.tensor_scalar(onehot_src[:, ds((n % 2) * P, P)], iota_src, src_f[:, ds(c, 1)],
                                                None, ALU.is_equal).then_inc(s_oh, 1)
                    dve.wait_ge(s_oh, (k + 1) * EC)
                    nc.vector.tensor_scalar(src_f, src_f, float(-P), None, ALU.add).then_inc(s_rel, 1)
                    dve.wait_ge(s_rel, k + 1)
                    dve.wait_ge(s_ohused, 2 + (k + 1) * EC)
                    for i in range(BPE):
                        w = min(CH, N - CH * i)
                        last = nc.vector.tensor_copy(adj[:, ds(k * N + CH * i, w)], ps[i][:, 0:w])
                    last.then_inc(s_evac, 1)

            @block.tensor
            def _(pe):
                pe.sem_inc(s_ohused, 2)

                def products(k, c, start, stop):
                    n = k * EC + c
                    pe.wait_ge(s_oh, n + 1)
                    for i in range(BPE):
                        w = min(CH, N - CH * i)
                        last = nc.tensor.matmul(ps[i][:, 0:w], onehot_src[:, ds((n % 2) * P, P)],
                                                onehot_dst[:, ds((n % 2) * NPAD + CH * i, w)], start=start, stop=stop)
                    last.then_inc(s_ohused, 1)
                    return last

                with pe.Fori(0, KT) as k:
                    pe.wait_ge(s_evac, k + 1)
                    products(k, 0, True, False)
                    with pe.Fori(1, EC - 1) as c:
                        products(k, c, False, False)
                    products(k, EC - 1, False, True)

        s_deg, s_degread, s_rdeg, s_rdegout, s_cr = (sem("s_deg"), sem("s_degread"), sem("s_rdeg"), sem("s_rdegout"),
                                                     sem("s_cr"))
        s_ones = sem("s_ones")
        ones = onehot_dst[:, 0:P]

        def width(j):
            return TAIL if isinstance(j, int) and j == NF else CH

        with nc.Block() as block:
            @block.vector
            def _(dve):
                nc.vector.memset(ones, 1.0).then_inc(s_ones, 1)
                for j in range(NCH):
                    w = width(j)
                    dve.wait_ge(s_deg, j + 1)
                    if j >= 1:
                        dve.wait_ge(s_rdegout, 16 * j)
                    nc.vector.tensor_scalar(scratch[:, 0:w], ps[j % 2][:, 0:w], 1.0, None, ALU.max).then_inc(s_degread, 1)
                    dve.wait_ge(s_degread, j + 1)
                    if j == NF:
                        nc.vector.reciprocal(rdeg_tail[:, :], scratch[:, 0:w])
                    else:
                        nc.vector.reciprocal(rdeg[:, :], scratch[:, 0:w]).then_inc(s_rdeg, 1)

            @block.tensor
            def _(pe):
                pe.wait_ge(s_ones, 1)
                for j in range(NCH):
                    w = width(j)
                    if j >= 2:
                        pe.wait_ge(s_degread, j - 1)
                    for k in range(KT):
                        last = nc.tensor.matmul(ps[j % 2][:, 0:w], ones, adj[:, k * N + j * CH:k * N + j * CH + w],
                                                start=(k == 0), stop=(k == KT - 1))
                    last.then_inc(s_deg, 1)

            @block.sync
            def _(sp):
                for j in range(NF):
                    sp.wait_ge(s_rdeg, j + 1)
                    sp.dma_start(rdeg_dram[j], rdeg[:, :]).then_inc(s_rdegout, 16)
                sp.wait_ge(s_rdegout, 16 * NF)

        def layernorm(nc, link, sqrt_ready, root_ready, act_n, eng, xt, xc, sq, a, p):
            sums, mean, var, root, inv, tmp = (stat[0:p, i, 0:a] for i in range(6))

            def over_d(t):
                return t.rearrange("p (a o) -> p a o", o=1).broadcast_to([p, a, D])

            link(nc.vector.tensor_reduce(sums, xt, AX.X, ALU.add))
            link(nc.vector.tensor_scalar(mean, sums, 1.0 / D, None, ALU.mult))
            link(nc.vector.tensor_tensor(xc, xt, over_d(mean), ALU.subtract))
            link(nc.vector.tensor_tensor(sq, xc, xc, ALU.mult))
            link(nc.vector.tensor_reduce(sums, sq, AX.X, ALU.add))
            nc.vector.tensor_scalar(var, sums, 1.0 / D, EPS, ALU.mult, ALU.add).then_inc(sqrt_ready, 1)
            eng.wait_ge(sqrt_ready, act_n)
            eng.wait_ge(root_ready, act_n)
            link(nc.vector.reciprocal(inv, root))
            link(nc.vector.tensor_tensor(tmp, var, inv, ALU.mult))
            link(nc.vector.tensor_tensor(root, root, tmp, ALU.add))
            link(nc.vector.tensor_scalar(root, root, 0.5, None, ALU.mult))
            link(nc.vector.reciprocal(inv, root))
            link(nc.vector.tensor_tensor(xc, xc, over_d(inv), ALU.mult))

        def parity(t):
            if isinstance(t, int):
                return t % 2
            assert t.out_of_modulus % 2 == 0
            return t.guaranteed_mod_val % 2

        def part(t, k, h):
            return ds(parity(t) * PW + k * 2 * D + h * D, D)

        def parts4(t, j, h, a, p):
            v = parts[0:p, ds(parity(t) * PW + j * TPC * 2 * D, a * 2 * D)].rearrange("p (a h d) -> p a h d", a=a, h=2)
            return v[:, :, h, :]

        def tiled(t, a, p):
            return t[0:p, 0:a * D].rearrange("p (a d) -> p a d", a=a)

        s_xin, s_xused, s_var, s_root, s_cl = sem("s_xin"), sem("s_xused"), sem("s_var"), sem("s_root"), sem("s_cl")
        s_hi0 = sem("s_hi0")
        s_zero = sem("s_zero")
        x_buf = hidden[:, 0, :]
        xc_buf = hidden[:, 1, :]
        sq_buf = scratch
        with nc.Block() as block:
            @block.sync
            def _(sp):
                for j in range(NCH):
                    a, p = (1, TAIL) if j == NF else (TPC, P)
                    if j >= 1:
                        sp.wait_ge(s_xused, j)
                    sp.dma_start(tiled(x_buf, a, p) if j < NF else x_buf[0:p, 0:D], node_rows(x, j)).then_inc(s_xin, 16)

            @block.scalar
            def _(act):
                for j in range(NCH):
                    a, p = (1, TAIL) if j == NF else (TPC, P)
                    act.wait_ge(s_var, j + 1)
                    nc.scalar.activation(stat[0:p, 3, 0:a], stat[0:p, 2, 0:a], ACT.Sqrt).then_inc(s_root, 1)

            @block.vector
            def _(dve):
                link = Chain(dve, s_cl)
                link(nc.vector.memset(parts[:, :], 0.0))
                link(nc.vector.memset(state[:, N:KT * P], 0.0))
                for j in range(NCH):
                    a, p = (1, TAIL) if j == NF else (TPC, P)
                    dve.wait_ge(s_xin, 16 * (j + 1))
                    layernorm(nc, link, s_var, s_root, j + 1, dve, tiled(x_buf, a, p), tiled(xc_buf, a, p),
                              tiled(sq_buf, a, p), a, p)
                    link(nc.vector.tensor_scalar(tiled(sq_buf, a, p), tiled(xc_buf, a, p), 0.0, LN_SCALE, ALU.max, ALU.mult))
                    link(nc.vector.tensor_copy(parts4(1, j, 0, a, p), tiled(sq_buf, a, p)))
                    ins = nc.vector.tensor_tensor(parts4(1, j, 1, a, p), tiled(sq_buf, a, p), parts4(1, j, 0, a, p),
                                                  ALU.subtract)
                    link.n += 0
                    ins.then_inc(s_xused, 1)
                    dve.wait_ge(s_xused, j + 1)

        def aggregate(eng, bank, t, j, wait_parts=None, between=None):
            w = width(j)
            for k in range(KT):
                if wait_parts is not None:
                    wait_parts(k)
                for h in range(2):
                    last = nc.tensor.matmul(bank[:, 0:w], parts[:, part(t, k, h)], adj[:, ds(j * CH + k * N, w)],
                                            start=(k == 0 and h == 0), stop=(k == KT - 1 and h == 1))
                if between is not None:
                    between(k)
            return last

        s_g, s_sum, s_y, s_yread, s_b0 = sem("s_g"), sem("s_sum"), sem("s_y"), sem("s_yread"), sem("s_b0")
        s_xin1, s_x1out, s_var1, s_root1, s_cf = (sem("s_xin1"), sem("s_x1out"), sem("s_var1"), sem("s_root1"),
                                                  sem("s_cf"))
        s_x1, s_ln, s_lnt, s_lntc, s_in, s_st, s_stt, s_hi, s_lo = (
            sem("s_x1"), sem("s_ln"), sem("s_lnt"), sem("s_lntc"), sem("s_in"), sem("s_st"), sem("s_stt"),
            sem("s_hi"), sem("s_lo"))
        x1_buf = diff
        with nc.Block() as block:
            @block.sync
            def _(sp):
                for j in range(NCH):
                    a, p = (1, TAIL) if j == NF else (TPC, P)
                    if j >= 1:
                        sp.wait_ge(s_x1, j)
                    sp.dma_start(tiled(x_buf, a, p) if j < NF else x_buf[0:p, 0:D], node_rows(x, j)).then_inc(s_xin1, 16)
                    sp.wait_ge(s_x1, j + 1)
                    sp.dma_start(node_rows(x1_dram, j), tiled(x1_buf, a, p) if j < NF else x1_buf[0:p, 0:D])\
                        .then_inc(s_x1out, 16)
                sp.wait_ge(s_x1out, 16 * NCH)

            @block.tensor
            def _(pe):
                for j in range(NCH):
                    w = width(j)
                    a, p = (1, TAIL) if j == NF else (TPC, P)
                    if j >= 2:
                        pe.wait_ge(s_sum, j - 1)
                    aggregate(pe, ps[j % 2], 1, j).then_inc(s_g, 1)
                    pe.wait_ge(s_sum, j + 1)
                    for i in range(a):
                        last = nc.tensor.matmul(ps[2][0:p, i * D:(i + 1) * D], agg[:, i * P:i * P + p], w0t[:, :],
                                                start=True, stop=True)
                    last.then_inc(s_y, 1)
                    pe.wait_ge(s_ln, j + 1)
                    for i in range(a):
                        last = nc.tensor.transpose(ps[3][:, i * P:i * P + p], xc_buf[0:p, i * D:(i + 1) * D],
                                                   ident[0:p, 0:p])
                    last.then_inc(s_lnt, 1)
                    pe.wait_ge(s_lntc, j + 1)
                    nc.tensor.matmul(ps[4][:, 0:w], w_in[:, :], agg[:, 0:w], start=True, stop=True).then_inc(s_in, 1)
                    pe.wait_ge(s_st, j + 1)
                    for i in range(a):
                        last = nc.tensor.transpose(ps[5][:, i * D:(i + 1) * D],
                                                   state[:, j * CH + i * P:j * CH + (i + 1) * P], ident[:, :])
                    last.then_inc(s_stt, 1)

            @block.scalar
            def _(act):
                for j in range(NCH):
                    w = width(j)
                    a, p = (1, TAIL) if j == NF else (TPC, P)
                    act.wait_ge(s_var1, j + 1)
                    nc.scalar.activation(stat[0:p, 3, 0:a], stat[0:p, 2, 0:a], ACT.Sqrt).then_inc(s_root1, 1)
                    act.wait_ge(s_lnt, j + 1)
                    nc.scalar.activation(agg[:, 0:w], ps[3][:, 0:w], ACT.Copy).then_inc(s_lntc, 1)
                    act.wait_ge(s_in, j + 1)
                    nc.scalar.activation(state[:, j * CH:j * CH + w], ps[4][:, 0:w], ACT.Tanh,
                                         bias=b_in_col[:, :]).then_inc(s_st, 1)
                    act.wait_ge(s_stt, j + 1)
                    nc.scalar.activation(parts4(0, j, 0, a, p), tiled(ps[5], a, p), ACT.Copy,
                                         scale=scale[0:p, 0:1]).then_inc(s_hi, 1)

            @block.vector
            def _(dve):
                link = Chain(dve, s_cf)
                for j in range(NCH):
                    w = width(j)
                    a, p = (1, TAIL) if j == NF else (TPC, P)
                    dve.wait_ge(s_g, j + 1)
                    nc.vector.tensor_scalar(agg[:, 0:w], ps[j % 2][:, 0:w], 1.0 / LN_SCALE, None, ALU.mult)\
                        .then_inc(s_sum, 1)
                    dve.wait_ge(s_y, j + 1)
                    dve.wait_ge(s_xin1, 16 * (j + 1))
                    if j >= 1:
                        dve.wait_ge(s_x1out, 16 * j)
                    link(nc.vector.tensor_tensor(tiled(x1_buf, a, p), tiled(ps[2], a, p), tiled(x_buf, a, p), ALU.add))
                    nc.vector.tensor_tensor(
                        tiled(x1_buf, a, p), tiled(x1_buf, a, p),
                        b0_row[0:p, :].rearrange("p (o d) -> p o d", o=1).broadcast_to([p, a, D]), ALU.add)\
                        .then_inc(s_x1, 1)
                    dve.wait_ge(s_x1, j + 1)
                    layernorm(nc, link, s_var1, s_root1, j + 1, dve, tiled(x1_buf, a, p), tiled(xc_buf, a, p),
                              tiled(sq_buf, a, p), a, p)
                    nc.vector.tensor_scalar(tiled(xc_buf, a, p), tiled(xc_buf, a, p), 0.0, None, ALU.max)\
                        .then_inc(s_ln, 1)
                    dve.wait_ge(s_hi, j + 1)
                    nc.vector.scalar_tensor_tensor(parts4(0, j, 1, a, p), tiled(ps[5], a, p), scale[0:p, 0:1],
                                                   parts4(0, j, 0, a, p), ALU.mult, ALU.subtract).then_inc(s_lo, 1)

        (t_parts, t_agg, t_aggs, t_hid, t_gelu, t_out, t_tanh, t_state, t_tr, t_hi, t_rdeg, t_cs,
         t_x1, t_fin, t_store, t_scale) = (
            sem("t_parts"), sem("t_agg"), sem("t_aggs"), sem("t_hid"), sem("t_gelu"),
            sem("t_out"), sem("t_tanh"), sem("t_state"), sem("t_tr"), sem("t_hi"), sem("t_rdeg"), sem("t_cs"),
            sem("t_x1"), sem("t_fin"), sem("t_store"), sem("t_scale"))
        HIDB, OUTB, TRB = (ps[3], ps[4]), ps[5], ps[6]
        LAST = STEPS - 1

        def agg_bank(j):
            return ps[2] if isinstance(j, int) and j == NF else ps[j % 2]

        def shape_of(j):
            return (1, TAIL) if j == NF else (TPC, P)

        def state_cols(j, i=0, n=None):
            return state[:, ds(j * CH + i * P, width(j) if n is None else n)]

        with nc.Block() as block:
            @block.sync
            def _(sp):
                def step(t):
                    for j in range(NF):
                        m = t * NF + j
                        if j >= 1:
                            sp.wait_ge(t_aggs, t * NCH + j)
                        elif not isinstance(t, int):
                            sp.wait_ge(t_aggs, t * NCH - 1)
                        sp.dma_start(rdeg[:, :], rdeg_dram[j]).then_inc(t_rdeg, 16)
                step(0)
                with sp.Fori(1, STEPS) as t:
                    step(t)
                for j in range(NCH):
                    a, p = shape_of(j)
                    n = LAST * NCH + j
                    if j == 0:
                        sp.wait_ge(t_gelu, 2 * STEPS * NCH)
                    else:
                        sp.wait_ge(t_fin, j)
                    sp.dma_start(tiled(scratch, a, p) if j < NF else scratch[0:p, 0:D], node_rows(x1_dram, j)).then_inc(t_x1, 16)
                    sp.wait_ge(t_fin, j + 1)
                    sp.dma_start(node_rows(out, j), tiled(rdeg, a, p) if j < NF else rdeg[0:p, 0:D]).then_inc(t_store, 16)
                sp.wait_ge(t_store, 16 * NCH)

            @block.tensor
            def _(pe):
                def chunk_sum(t, j, wait_parts=None, between=None):
                    n = t * NCH + j
                    if not (isinstance(n, int) and n < 2):
                        wait(pe, t_aggs, n - 1)
                    aggregate(pe, agg_bank(j), t, j, wait_parts, between).then_inc(t_agg, 1)

                def project_up(t, j):
                    n = t * NCH + j
                    w = width(j)
                    wait(pe, t_aggs, n + 1)
                    src_t = agg_tail if j == NF else agg
                    for half in range(2):
                        wait(pe, t_gelu, 2 * n)
                        nc.tensor.matmul(HIDB[half][:, 0:w], w1[:, half * P:(half + 1) * P], src_t[:, 0:w],
                                         start=True, stop=True).then_inc(t_hid, 1)

                def project_down(t, j):
                    n = t * NCH + j
                    w = width(j)
                    wait(pe, t_tanh, n)
                    for half in range(2):
                        wait(pe, t_gelu, 2 * n + 1 + half)
                        last = nc.tensor.matmul(OUTB[:, 0:w], w2[:, half, :], hidden[:, half, 0:w],
                                                start=(half == 0), stop=(half == 1))
                    last.then_inc(t_out, 1)

                def to_nodes(t, j, final=False):
                    n = t * NCH + j
                    a, p = shape_of(j)
                    wait(pe, t_state, n + 1)
                    if final:
                        if j >= 1:
                            wait(pe, t_fin, j)
                        else:
                            wait(pe, t_parts, LAST * NCH)
                    else:
                        wait(pe, t_parts, n)
                    for i in range(a):
                        last = nc.tensor.transpose(TRB[:, i * D:(i + 1) * D], state_cols(j, i, P), ident[:, :])
                    last.then_inc(t_tr, 1)

                def middle(t, final=False):
                    for j in range(1, NCH):
                        def between(k, j=j):
                            if k == 3:
                                project_up(t, j - 1)
                            if k == 11:
                                project_down(t, j - 1)
                            if k == 19 and not final:
                                to_nodes(t, j - 1)
                        chunk_sum(t, j, between=between if j < NF else None)

                def bridge(t):
                    def wait_parts(k):
                        if k == 0:
                            wait(pe, t_parts, t * NCH + NF - 1)
                        if k == (NF - 1) * TPC:
                            wait(pe, t_parts, t * NCH + NF)
                        if k == NF * TPC:
                            wait(pe, t_parts, (t + 1) * NCH)

                    def between(k):
                        if k == 1:
                            project_up(t, NF - 1)
                        if k == 6:
                            project_down(t, NF - 1)
                        if k == 7:
                            project_up(t, NF)
                        if k == 10:
                            to_nodes(t, NF - 1)
                        if k == 15:
                            project_down(t, NF)
                        if k == 19:
                            to_nodes(t, NF)
                    chunk_sum(t + 1, 0, wait_parts, between)

                chunk_sum(0, 0)
                middle(0)
                bridge(0)
                with pe.Fori(0, (LAST - 1) // 2) as pair:
                    for t in (pair * 2 + 1, pair * 2 + 2):
                        middle(t)
                        bridge(t)
                middle(LAST, True)
                for j in (NF - 1, NF):
                    project_up(LAST, j)
                    project_down(LAST, j)
                for j in range(NCH):
                    to_nodes(LAST, j, True)

            @block.scalar
            def _(act):
                def dense(t, j, final=False):
                    n = t * NCH + j
                    w = width(j)
                    for half in range(2):
                        wait(act, t_hid, 2 * n + 1 + half)
                        wait(act, t_out, n)
                        nc.scalar.activation(hidden[:, half, 0:w], HIDB[half][:, 0:w], ACT.Gelu,
                                             bias=b1_col[:, half:half + 1]).then_inc(t_gelu, 1)
                    wait(act, t_out, n + 1)
                    wait(act, t_state, n)
                    nc.scalar.activation(diff[:, 0:w], OUTB[:, 0:w], ACT.Tanh, bias=b2_col[:, :]).then_inc(t_tanh, 1)
                    if not final:
                        a, p = shape_of(j)
                        wait(act, t_tr, n + 1)
                        nc.scalar.activation(parts4(t + 1, j, 0, a, p), tiled(TRB, a, p), ACT.Copy,
                                             scale=step_scale[0:p, 1:2]).then_inc(t_hi, 1)

                for j in range(NCH):
                    dense(0, j)
                with act.Fori(0, (LAST - 1) // 2) as pair:
                    for t in (pair * 2 + 1, pair * 2 + 2):
                        for j in range(NCH):
                            dense(t, j)
                for j in range(NCH):
                    dense(LAST, j, True)

            @block.vector
            def _(dve):
                def scale_out(t, j):
                    n = t * NCH + j
                    w = width(j)
                    wait(dve, t_agg, n + 1)
                    if j < NF:
                        wait(dve, t_rdeg, 16 * (t * NF + j + 1))
                    wait(dve, t_hid, 2 * (n - NF) if j == NF else 2 * n)
                    dst_t, r = (agg_tail, rdeg_tail) if j == NF else (agg, rdeg)
                    nc.vector.scalar_tensor_tensor(dst_t[:, 0:w], agg_bank(j)[:, 0:w], step_scale[:, 0:1], r[:, 0:w],
                                                   ALU.mult, ALU.mult).then_inc(t_aggs, 1)

                def dense(t, j, final):
                    n = t * NCH + j
                    w = width(j)
                    wait(dve, t_tanh, n + 1)
                    nc.vector.scalar_tensor_tensor(diff[:, 0:w], state_cols(j), decay[:, 1:2], diff[:, 0:w],
                                                   ALU.mult, ALU.add).then_inc(t_cs, 1)
                    wait(dve, t_cs, n + 1)
                    nc.vector.scalar_tensor_tensor(state_cols(j), diff[:, 0:w], DT, state_cols(j),
                                                   ALU.mult, ALU.add).then_inc(t_state, 1)
                    a, p = shape_of(j)
                    if not final:
                        wait(dve, t_hi, n + 1)
                        nc.vector.scalar_tensor_tensor(parts4(t + 1, j, 1, a, p), tiled(TRB, a, p),
                                                       step_scale[0:p, 1:2], parts4(t + 1, j, 0, a, p),
                                                       ALU.mult, ALU.subtract).then_inc(t_parts, 1)

                def finish(t, j):
                    a, p = shape_of(j)
                    wait(dve, t_tr, t * NCH + j + 1)
                    wait(dve, t_x1, 16 * (j + 1))
                    if j >= 1:
                        wait(dve, t_store, 16 * j)
                    nc.vector.tensor_tensor(tiled(rdeg, a, p), tiled(scratch, a, p), tiled(TRB, a, p), ALU.add)\
                        .then_inc(t_fin, 1)

                def step(t, final=False):
                    wait(dve, t_aggs, t * NCH)
                    wait(dve, t_parts, t * NCH)
                    nc.vector.tensor_copy(step_scale[:, 0:1], unscale[:, ds(t, 1)])
                    nc.vector.tensor_copy(step_scale[:, 1:2], scale[:, ds(t + 1, 1)]).then_inc(t_scale, 1)
                    wait(dve, t_scale, t + 1)
                    scale_out(t, 0)
                    for j in range(1, NF):
                        dense(t, j - 1, final)
                        scale_out(t, j)
                    scale_out(t, NF)
                    dense(t, NF - 1, final)
                    dense(t, NF, final)

                step(0)
                with dve.Fori(0, (LAST - 1) // 2) as pair:
                    step(pair * 2 + 1)
                    step(pair * 2 + 2)
                step(LAST, True)
                for j in range(NCH):
                    finish(LAST, j)


_INS = ['x', 'src', 'dst', 'L0_gnn_W', 'L0_gnn_b', 'L1_gnn_W_in', 'L1_gnn_b_in', 'L1_gnn_W1', 'L1_gnn_b1', 'L1_gnn_W2',
        'L1_gnn_b2', 'L1_gnn_clearance']


def kernel(**inputs):
    import numpy as _np
    import concourse.bacc as _bacc
    from concourse import mybir as _mybir
    from concourse.bass_utils import run_bass_kernel_spmd as _run

    nc = _bacc.Bacc("TRN2", target_bir_lowering=False, num_devices=1)
    arrays, args = {}, []
    for name in _INS:
        a = _np.ascontiguousarray(inputs[name])
        arrays[f"in_{name}"] = a
        args.append(nc.dram_tensor(f"in_{name}", a.shape, _mybir.dt.from_np(a.dtype), kind="ExternalInput").ap())
    shape = inputs['x'].shape
    args.append(nc.dram_tensor("out_0", shape, _mybir.dt.float32, kind="ExternalOutput").ap())
    graph_layers_kernel(nc, *args)
    r = _run(nc, [arrays], core_ids=[0])
    return r.results[0]["out_0"]
```

```python
from contextlib import ExitStack

import concourse.bass as bass
from concourse import mybir

ALU = mybir.AluOpType
ACT = mybir.ActivationFunctionType
AX = mybir.AxisListType
F32 = mybir.dt.float32
F16 = mybir.dt.float16
BF16 = mybir.dt.bfloat16
I32 = mybir.dt.int32

P = 128
STEPS = 12
DT = 6.0 / STEPS
EPS = 1e-5
LN_SCALE = 2.0 ** 11
J = 7
CAP = 3
CHAINS = 16
BIG = 2.0 ** 16
CH = 512
ds = bass.ds


def wait(eng, sem, value):
    if not (isinstance(value, int) and value <= 0):
        eng.wait_ge(sem, value)


class Chain:

    def __init__(self, eng, sem, base=0):
        self.eng, self.sem, self.base, self.n = eng, sem, base, 0

    def __call__(self, ins):
        ins.then_inc(self.sem, 1)
        self.n += 1
        self.eng.wait_ge(self.sem, self.base + self.n)


def graph_layers_kernel(nc, x, src, dst, W0, b0, W_in, b_in, W1, b1, W2, b2, clearance, out):
    N, D = x.shape
    E = src.shape[0]
    HID = W1.shape[1]
    KT = -(-N // P)
    LASTK = N - (KT - 1) * P
    NF = N // CH
    TAIL = N - NF * CH
    TPC = CH // P
    ROUNDS = -(-E // (P * CHAINS))
    EC = ROUNDS * CHAINS
    NPAD = N + N % 2
    WJ = -(-N // J)
    WJE = WJ + WJ % 2
    B = KT * J
    BS = B + B % 2
    SLOTS = B * CAP
    SETS = CHAINS // 4
    NCH = NF + 1
    PW = KT * 2 * D
    assert E % EC == 0 and D == P and HID == 2 * D and NF * TPC == KT - 1 and TAIL == LASTK

    rdeg_dram = nc.dram_tensor("rdeg_scratch", [NCH, P, CH], F32, kind="Internal").ap()
    x1_dram = nc.dram_tensor("x1_scratch", [N, D], F32, kind="Internal").ap()

    def node_rows(dram, j):
        if isinstance(j, int) and j == NF:
            return dram[NF * CH:N, :]
        return dram[ds(j * CH, CH), :].rearrange("(a p) d -> p a d", p=P)

    with ExitStack() as ctx:
        def sb(name, shape, dt=F32):
            return ctx.enter_context(nc.sbuf_tensor(name, shape, dt))

        def sem(name):
            return ctx.enter_context(nc.semaphore(name))

        adj = sb("adj", [P, KT * N], F16)
        parts = sb("parts", [P, 2 * PW], F16)
        state = sb("state", [P, KT * P])
        rdeg = sb("rdeg", [P, CH])
        rdeg_tail = sb("rdeg_tail", [P, TAIL])
        agg = sb("agg", [P, CH])
        agg_tail = sb("agg_tail", [P, TAIL])
        hidden = sb("hidden", [P, 2, CH])
        scratch = sb("scratch", [P, CH])
        diff = sb("diff", [P, CH])
        w1 = sb("w1", [P, HID])
        w2 = sb("w2", [P, 2, D])
        w_in = sb("w_in", [P, D])
        w0t = sb("w0t", [P, D])
        b0_row = sb("b0_row", [P, D])
        ident = sb("ident", [P, P])
        b1_col = sb("b1_col", [P, 2])
        b2_col = sb("b2_col", [P, 1])
        b_in_col = sb("b_in_col", [P, 1])
        decay = sb("decay", [P, 2])
        bound = sb("bound", [P, STEPS + 1])
        scale = sb("scale", [P, STEPS + 1])
        unscale = sb("unscale", [P, STEPS + 1])
        step_scale = sb("step_scale", [P, 2])
        stat = sb("stat", [P, 8, TPC])
        overflow = sb("overflow", [P, 1], I32)

        def carver(region, dt, limit):
            at = [0]

            def carve(n, view=None):
                words = n if dt == F32 else n + n % 2
                start, at[0] = at[0], at[0] + words
                assert at[0] <= limit
                return region[:, start:start + n]
            return carve

        carve_f32 = carver(state, F32, KT * P)
        carve_f16 = carver(parts, F16, 2 * PW)

        psum = ctx.enter_context(nc.psum_tensor("psum", [P, 8, CH], F32))
        ps = [psum[:, i, :] for i in range(8)]

        src_w, dst_w, rank, code, low, mid = (carve_f32(EC) for _ in range(6))
        src_i, dst_i, rank_i, code_i = (v.bitcast(I32) for v in (src_w, dst_w, rank, code))
        table = carve_f16(2 * 2 * SLOTS).bitcast(F32).rearrange("p (h n) -> p h n", h=2)
        iota_b = carve_f16(B).bitcast(BF16)
        iota_slot, iota_row = carve_f16(SLOTS), carve_f16(P)
        iota_src1, iota_mid1 = carve_f16(P), carve_f16(WJ)
        tri, eye, big, negbig = (carve_f16(P).bitcast(BF16) for _ in range(4))
        chain_n = carve_f16(CHAINS * B).bitcast(BF16).rearrange("p (q b) -> p q b", q=CHAINS)
        half_n = carve_f16(2 * B).bitcast(BF16).rearrange("p (q b) -> p q b", q=2)
        bucket_oh = adj[:, 0:EC * BS].bitcast(BF16).rearrange("p (q r b) -> p q r b", q=CHAINS, b=BS)

        def chain_tiles(i, r):
            if isinstance(r, int):
                return bucket_oh[:, 2 * i:2 * i + 2, r, 0:B]
            return bucket_oh[:, 2 * i:2 * i + 2, ds(r, 1), 0:B].rearrange("p q o b -> p q (o b)")
        all_ones, flag_bf16 = carve_f16(P).bitcast(BF16), carve_f16(1).bitcast(BF16)
        adj_bf16 = adj[:, :].bitcast(BF16)
        rank_by_chain = rank.rearrange("p (q r) -> p q r", r=ROUNDS)
        hidden_f16 = hidden[:, :, :].rearrange("p a n -> p (a n)").bitcast(F16)
        scratch_f16, diff_f16, agg_f16 = (v[:, :].bitcast(F16) for v in (scratch, diff, agg))
        RING = 4
        SLE = SLOTS + SLOTS % 2
        slot_oh = [hidden_f16[:, i * SLE:i * SLE + SLOTS] for i in range(3)] + [scratch_f16[:, 0:SLOTS]]
        row_src = [agg_f16[:, i * P:(i + 1) * P] for i in range(RING)]
        row_mid = [agg_f16[:, (RING + i) * P:(RING + i + 1) * P] for i in range(RING)]
        RING7 = J
        mid_oh = [hidden_f16[:, i * WJE:i * WJE + WJ] for i in range(4)] + [scratch_f16[:, i * WJE:i * WJE + WJ] for i in range(2)] + \
                 [diff_f16[:, 0:WJ]]
        src_oh = [agg_f16[:, i * P:(i + 1) * P] for i in range(RING7)]

        s_edges, s_w, s_fill, s_iota, s_id, s_const = (sem("s_edges"), sem("s_w"), sem("s_fill"), sem("s_iota"),
                                                       sem("s_id"), sem("s_const"))
        s_cd, s_w0t, s_codes = sem("s_cd"), sem("s_w0t"), sem("s_codes")
        s_tri = sem("s_tri")
        PROWS = E // EC
        with nc.Block() as block:
            @block.sync
            def _(sp):
                sp.wait_ge(s_fill, 2)
                for dram, tile in ((src, src_i), (dst, dst_i)):
                    sp.dma_start(tile[0:PROWS, :], dram[0:PROWS * EC].rearrange("(p c) -> p c", c=EC)).then_inc(s_edges, 16)
                sp.dma_start(agg[:, 0:D], W0).then_inc(s_w, 16)
                sp.dma_start(w_in[:, :], W_in).then_inc(s_w, 16)
                sp.dma_start(w1[:, :], W1).then_inc(s_w, 16)
                sp.dma_start(w2[:, :, :], W2.rearrange("(h p) n -> p h n", p=P)).then_inc(s_w, 16)
                sp.dma_start(b0_row[:, :], b0.rearrange("(a n) -> a n", a=1).broadcast_to([P, D])).then_inc(s_w, 16)
                with nc.allow_non_contiguous_dma("bias columns"):
                    sp.dma_start(b1_col[:, :], b1.rearrange("(h p) -> p h", p=P)).then_inc(s_w, 16)
                    sp.dma_start(b2_col[:, :], b2.rearrange("(p a) -> p a", a=1)).then_inc(s_w, 16)
                    sp.dma_start(b_in_col[:, :], b_in.rearrange("(p a) -> p a", a=1)).then_inc(s_w, 16)
                    sp.dma_start(decay[:, 0:1], clearance.rearrange("(a n) -> a n", a=1).broadcast_to([P, 1])).then_inc(s_w, 16)

            @block.gpsimd
            def _(pool):
                pool.memset(src_i, -P * (KT + 1)).then_inc(s_fill, 1)
                pool.memset(dst_i, 0).then_inc(s_fill, 1)
                for tile, n, base in ((iota_b, B, 0), (iota_slot, SLOTS, 0), (iota_row, P, 0), (iota_src1, P, 1),
                                      (iota_mid1, WJ, 1)):
                    pool.iota(tile, [[1, n]], base=base, channel_multiplier=0,
                              allow_small_or_imprecise_dtypes=True).then_inc(s_iota, 1)
                pool.memset(ident[:, :], 0.0).then_inc(s_id, 1)
                pool.memset(tri, 1.0).then_inc(s_id, 1)
                pool.wait_ge(s_id, 2)
                pool.affine_select(out=ident[:, :], in_=ident[:, :], compare_op=ALU.not_equal, fill=1.0, base=0,
                                   pattern=[[-1, P]], channel_multiplier=1).then_inc(s_const, 1)
                pool.affine_select(out=tri, in_=tri, compare_op=ALU.is_ge, fill=0.0, base=-1,
                                   pattern=[[1, P]], channel_multiplier=-1).then_inc(s_tri, 1)

            @block.vector
            def _(dve):
                link = Chain(dve, s_cd)
                dve.wait_ge(s_const, 1)
                for tile, factor in ((eye, 1.0), (big, BIG), (negbig, -BIG)):
                    nc.vector.tensor_scalar(tile, ident[:, :], factor, None, ALU.mult)
                dve.wait_ge(s_edges, 32)
                link(nc.vector.tensor_copy(rank, dst_i))
                link(nc.vector.tensor_scalar(mid, rank, -(J - 1) / 2.0, 1.0 / J, ALU.add, ALU.mult))
                link(nc.vector.tensor_scalar(mid, mid, 1.5 * 2.0 ** 23, -1.5 * 2.0 ** 23, ALU.add, ALU.add))
                link(nc.vector.scalar_tensor_tensor(rank, mid, -float(J), rank, ALU.mult, ALU.add))
                link(nc.vector.tensor_scalar(mid, mid, 1.0, None, ALU.add))
                link(nc.vector.tensor_scalar(code_i, src_i, P - 1, None, ALU.bitwise_and))
                link(nc.vector.tensor_scalar(low, code_i, 1.0, None, ALU.add))
                link(nc.vector.tensor_scalar(code_i, src_i, 7, None, ALU.arith_shift_right))
                link(nc.vector.tensor_copy(dst_w, code_i))
                link(nc.vector.scalar_tensor_tensor(code, dst_w, float(J), rank, ALU.mult, ALU.add))
                dve.wait_ge(s_w, 9 * 16)
                link(nc.vector.tensor_scalar(decay[:, 1:2], decay[:, 0:1], 0.0, -1.0, ALU.max, ALU.mult))
                link(nc.vector.tensor_scalar(stat[:, 0, 0:1], decay[:, 1:2], DT, 1.0, ALU.mult, ALU.add))
                link(nc.vector.tensor_scalar(stat[:, 0, 1:2], stat[:, 0, 0:1], -1.0, None, ALU.mult))
                link(nc.vector.tensor_tensor(stat[:, 0, 0:1], stat[:, 0, 0:1], stat[:, 0, 1:2], ALU.max))
                link(nc.vector.memset(bound[:, 0:1], 1.0))
                for t in range(STEPS):
                    link(nc.vector.tensor_scalar(bound[:, t + 1:t + 2], bound[:, t:t + 1], stat[:, 0, 0:1], DT,
                                                 ALU.mult, ALU.add))
                link(nc.vector.tensor_scalar(unscale[:, :].bitcast(I32), bound[:, :].bitcast(I32), 0x7F800000, None,
                                             ALU.bitwise_and))
                link(nc.vector.tensor_scalar(unscale[:, :], unscale[:, :], 2.0 ** -14, None, ALU.mult))
                link(nc.vector.reciprocal(scale[:, :], unscale[:, :]))
                dve.wait_ge(s_w0t, 1)
                nc.vector.tensor_copy(w0t[:, :], ps[0][:, 0:D])

            @block.tensor
            def _(pe):
                pe.wait_ge(s_w, 9 * 16)
                pe.wait_ge(s_const, 1)
                nc.tensor.transpose(ps[0][:, 0:D], agg[:, 0:D], ident[:, :]).then_inc(s_w0t, 1)

        s_boh, s_cnt, s_cntc, s_half, s_halfc, s_base, s_round, s_read = (
            sem("s_boh"), sem("s_cnt"), sem("s_cntc"), sem("s_half"), sem("s_halfc"), sem("s_base"), sem("s_round"),
            sem("s_read"))
        s_pos, s_flag, s_flagc = sem("s_pos"), sem("s_flag"), sem("s_flagc")
        pair_of = [psum[:, i, 0:2 * B].rearrange("p (q b) -> p q b", q=2) for i in range(8)]
        UNROLL = 5
        with nc.Block() as block:
            @block.vector
            def _(dve):
                with dve.Fori(0, EC // UNROLL) as g:
                    for u in range(UNROLL):
                        nc.vector.tensor_scalar(adj_bf16[:, ds(g * (UNROLL * BS) + u * BS, B)], iota_b,
                                                code[:, ds(g * UNROLL + u, 1)], None, ALU.is_equal).then_inc(s_boh, 1)
                def read(r, s):
                    dve.wait_ge(s_round, SETS * r + s + 1)
                    nc.vector.tensor_reduce(
                        rank_by_chain[:, 4 * s:4 * s + 4, ds(r, 1)].rearrange("p q o -> p (q o)"),
                        psum[:, 2 * s:2 * s + 2, 0:2 * B].rearrange("p i (q b) -> p i q b", q=2),
                        AX.X, ALU.max).then_inc(s_read, 1)

                with dve.Fori(0, ROUNDS) as r:
                    for s in range(SETS):
                        read(r, s)
                dve.wait_ge(s_read, SETS * ROUNDS)
                link = Chain(dve, s_pos)
                link(nc.vector.tensor_scalar(dst_w, rank, -BIG, None, ALU.add))
                link(nc.vector.tensor_copy(rank_i, dst_w))
                link(nc.vector.tensor_scalar(src_w, dst_w, CAP * P - 0.5, None, ALU.is_gt))
                link(nc.vector.tensor_reduce(stat[:, 1, 0:1], src_w, AX.X, ALU.add))
                link(nc.vector.tensor_scalar(dst_w, dst_w, -0.5, None, ALU.is_gt))
                link(nc.vector.tensor_tensor(src_w, dst_w, src_w, ALU.subtract))
                link(nc.vector.tensor_scalar(dst_i, rank_i, 7, None, ALU.arith_shift_right))
                link(nc.vector.tensor_scalar(rank_i, rank_i, P - 1, None, ALU.bitwise_and))
                link(nc.vector.tensor_scalar(code, code, float(CAP), 1.0, ALU.mult, ALU.add))
                link(nc.vector.tensor_tensor(code, code, dst_i, ALU.add))
                link(nc.vector.tensor_tensor(code, code, src_w, ALU.mult))
                link(nc.vector.tensor_scalar(code, code, -1.0, None, ALU.add))
                link(nc.vector.tensor_copy(dst_w, rank_i))
                link(nc.vector.tensor_copy(rank, dst_w))
                link(nc.vector.tensor_copy(flag_bf16, stat[:, 1, 0:1]))
                nc.vector.memset(all_ones, 1.0).then_inc(s_flag, 1)
                dve.wait_ge(s_flag, 2)
                nc.vector.tensor_copy(overflow[:, :], ps[7][:, 0:1]).then_inc(s_flagc, 1)

            @block.tensor
            def _(pe):
                for i in range(CHAINS // 2):
                    for r in range(ROUNDS):
                        pe.wait_ge(s_boh, (2 * i + 1) * ROUNDS + r + 1)
                        last = nc.tensor.matmul(pair_of[i], eye, bucket_oh[:, 2 * i:2 * i + 2, r, 0:B],
                                                start=(r == 0), stop=(r == ROUNDS - 1))
                    last.then_inc(s_cnt, 1)
                pe.wait_ge(s_cntc, CHAINS // 2)
                for h in range(2):
                    for q in range(CHAINS // 2):
                        last = nc.tensor.matmul(ps[h][:, 0:B], eye, chain_n[:, h * (CHAINS // 2) + q, :],
                                                start=(q == 0), stop=(q == CHAINS // 2 - 1))
                    last.then_inc(s_half, 1)
                pe.wait_ge(s_halfc, 2)

                def both(v):
                    return v.rearrange("p (o b) -> p o b", o=1).broadcast_to([P, 2, B])

                for i in range(CHAINS // 2):
                    nc.tensor.matmul(pair_of[i], tri, both(half_n[:, 0, :]), start=True, stop=False)
                    for q in range(2 * i):
                        nc.tensor.matmul(pair_of[i], eye, both(chain_n[:, q, :]), start=False, stop=False)
                    nc.tensor.matmul(psum[:, i, B:2 * B], eye, chain_n[:, 2 * i, :], start=False, stop=False)
                    nc.tensor.matmul(pair_of[i], tri, both(half_n[:, 1, :]), start=False, stop=True)

                def mark(s, r):
                    for i in (2 * s, 2 * s + 1):
                        last = nc.tensor.matmul(pair_of[i], big, chain_tiles(i, r), start=False, stop=True,
                                                skip_group_check=True)
                    last.then_inc(s_round, 1)

                for s in range(SETS):
                    mark(s, 0)

                with pe.Fori(1, ROUNDS) as r:
                    for s in range(SETS):
                        pe.wait_ge(s_read, SETS * r - SETS + s + 1)
                        for i in (2 * s, 2 * s + 1):
                            nc.tensor.matmul(pair_of[i], negbig, chain_tiles(i, r - 1), start=False, stop=False,
                                             skip_group_check=True)
                            nc.tensor.matmul(pair_of[i], eye, chain_tiles(i, r - 1), start=False, stop=False,
                                             skip_group_check=True)
                        mark(s, r)
                pe.wait_ge(s_flag, 1)
                pe.wait_ge(s_read, SETS * ROUNDS)
                nc.tensor.matmul(ps[7][:, 0:1], all_ones, flag_bf16, start=True, stop=True).then_inc(s_flag, 1)

            @block.scalar
            def _(act):
                for i in range(CHAINS // 2):
                    act.wait_ge(s_cnt, i + 1)
                    nc.scalar.activation(chain_n[:, 2 * i:2 * i + 2, :], pair_of[i], ACT.Copy).then_inc(s_cntc, 1)
                for h in range(2):
                    act.wait_ge(s_half, h + 1)
                    nc.scalar.activation(half_n[:, h, :], ps[h][:, 0:B], ACT.Copy).then_inc(s_halfc, 1)

        s_soh, s_sused = sem("s_soh"), sem("s_sused")
        CUT = [(0, SLOTS // 2), (SLOTS // 2, SLOTS)]
        with nc.Block() as block:
            @block.vector
            def _(dve):
                with dve.Fori(0, EC // RING) as g:
                    for u in range(RING):
                        dve.wait_ge(s_sused, g * RING + u + 1)
                        c = g * RING + u
                        nc.vector.tensor_scalar(slot_oh[u], iota_slot, code[:, ds(c, 1)], None, ALU.is_equal)
                        nc.vector.tensor_scalar(row_src[u], iota_row, rank[:, ds(c, 1)], low[:, ds(c, 1)],
                                                ALU.is_equal, ALU.mult)
                        nc.vector.tensor_scalar(row_mid[u], iota_row, rank[:, ds(c, 1)], mid[:, ds(c, 1)],
                                                ALU.is_equal, ALU.mult).then_inc(s_soh, 1)
                dve.wait_ge(s_sused, RING + EC)
                for h in range(2):
                    for i, (a, b) in enumerate(CUT):
                        nc.vector.tensor_copy(table[:, h, a:b], ps[2 * h + i][:, 0:b - a])

            @block.tensor
            def _(pe):
                pe.sem_inc(s_sused, RING)

                def products(g, first=False, final=False):
                    for u in range(RING):
                        pe.wait_ge(s_soh, g * RING + u + 1)
                        for h, rows in ((0, row_src), (1, row_mid)):
                            for i, (a, b) in enumerate(CUT):
                                last = nc.tensor.matmul(ps[2 * h + i][:, 0:b - a], rows[u], slot_oh[u][:, a:b],
                                                        start=(first and u == 0), stop=(final and u == RING - 1))
                        last.then_inc(s_sused, 1)

                products(0, first=True)
                with pe.Fori(1, EC // RING - 1) as g:
                    products(g)
                products(EC // RING - 1, final=True)

        s_moh, s_mused, s_bank, s_bankfree = sem("s_moh"), sem("s_mused"), sem("s_bank"), sem("s_bankfree")
        TPK = J * CAP
        with nc.Block() as block:
            @block.vector
            def _(dve):
                with dve.Fori(0, KT) as k:
                    for i in range(TPK):
                        dve.wait_ge(s_mused, k * TPK + i + 1)
                        nc.vector.tensor_scalar(mid_oh[i % J], iota_mid1, table[:, 1, ds(k * TPK + i, 1)], None,
                                                ALU.is_equal)
                        nc.vector.tensor_scalar(src_oh[i % J], iota_src1, table[:, 0, ds(k * TPK + i, 1)], None,
                                                ALU.is_equal).then_inc(s_moh, 1)

            @block.tensor
            def _(pe):
                pe.sem_inc(s_mused, J)
                with pe.Fori(0, KT) as k:
                    for i in range(TPK):
                        j = i // CAP
                        if i % CAP == 0:
                            pe.wait_ge(s_bankfree, k * J + j + 1)
                        pe.wait_ge(s_moh, k * TPK + i + 1)
                        ins = nc.tensor.matmul(ps[j][:, 0:WJ], src_oh[i % J], mid_oh[i % J],
                                               start=(i % CAP == 0), stop=(i % CAP == CAP - 1))
                        ins.then_inc(s_mused, 1)

            @block.scalar
            def _(act):
                act.sem_inc(s_bankfree, J)
                with act.Fori(0, KT) as k:
                    for j in range(J):
                        act.wait_ge(s_mused, k * TPK + (j + 1) * CAP + J)
                        wj = (N - j + J - 1) // J
                        nc.scalar.activation(adj[:, ds(k * N + j, wj, J)], ps[j][:, 0:wj], ACT.Copy)\
                            .then_inc(s_bankfree, 1)

        onehot_dst = parts[:, 0:2 * NPAD]
        iota_dst = parts[:, 2 * NPAD:2 * NPAD + N]
        src_f, dst_f = state[:, 0:EC], state[:, EC:2 * EC]
        src_g, dst_g = state[:, 2 * EC:3 * EC].bitcast(I32), state[:, 3 * EC:4 * EC].bitcast(I32)
        onehot_src = state[:, 4 * EC:4 * EC + P].bitcast(F16)
        iota_g = state[:, 4 * EC + P:4 * EC + P + P // 2].bitcast(F16)
        g_fill, g_edges, g_iota, g_edge_f = sem("g_fill"), sem("g_edges"), sem("g_iota"), sem("g_edge_f")
        s_oh, s_ohused, s_evac, s_rel = sem("s_oh"), sem("s_ohused"), sem("s_evac"), sem("s_rel")
        BPE = -(-N // CH)

        def overflowed(eng):
            return eng.If(eng.value_load(overflow[0:1, 0:1], min_val=0, max_val=1 << 30) > 0)

        with nc.Block() as block:
            @block.sync
            def _(sp):
                with overflowed(sp):
                    sp.wait_ge(g_fill, 2)
                    for dram, tile in ((src, src_g), (dst, dst_g)):
                        sp.dma_start(tile[0:PROWS, :], dram[0:PROWS * EC].rearrange("(p c) -> p c", c=EC))\
                            .then_inc(g_edges, 16)

            @block.gpsimd
            def _(pool):
                with overflowed(pool):
                    pool.memset(src_g, -1).then_inc(g_fill, 1)
                    pool.memset(dst_g, 0).then_inc(g_fill, 1)
                    pool.iota(iota_dst, [[1, N]], base=-(N // 2), channel_multiplier=0,
                              allow_small_or_imprecise_dtypes=True).then_inc(g_iota, 1)
                    pool.iota(iota_g, [[1, P]], base=0, channel_multiplier=0,
                              allow_small_or_imprecise_dtypes=True).then_inc(g_iota, 1)

            @block.vector
            def _(dve):
                with overflowed(dve):
                    dve.wait_ge(g_edges, 32)
                    dve.wait_ge(g_iota, 2)
                    nc.vector.tensor_copy(src_f, src_g).then_inc(g_edge_f, 1)
                    nc.vector.tensor_copy(dst_f, dst_g).then_inc(g_edge_f, 1)
                    dve.wait_ge(g_edge_f, 2)
                    nc.vector.tensor_scalar(dst_f, dst_f, float(-(N // 2)), None, ALU.add).then_inc(g_edge_f, 1)
                    dve.wait_ge(g_edge_f, 3)
                    dve.sem_inc(s_evac, 1)
                    with dve.Fori(0, KT) as k:
                        with dve.Fori(0, EC) as c:
                            n = k * EC + c
                            dve.wait_ge(s_ohused, n + 1)
                            nc.vector.tensor_scalar(onehot_dst[:, ds((n % 2) * NPAD, N)], iota_dst,
                                                    dst_f[:, ds(c, 1)], None, ALU.is_equal)
                            nc.vector.tensor_scalar(onehot_src[:, ds((n % 2) * P, P)], iota_g, src_f[:, ds(c, 1)],
                                                    None, ALU.is_equal).then_inc(s_oh, 1)
                        dve.wait_ge(s_oh, (k + 1) * EC)
                        nc.vector.tensor_scalar(src_f, src_f, float(-P), None, ALU.add).then_inc(s_rel, 1)
                        dve.wait_ge(s_rel, k + 1)
                        dve.wait_ge(s_ohused, 2 + (k + 1) * EC)
                        for i in range(BPE):
                            w = min(CH, N - CH * i)
                            last = nc.vector.tensor_copy(adj[:, ds(k * N + CH * i, w)], ps[i][:, 0:w])
                        last.then_inc(s_evac, 1)

            @block.tensor
            def _(pe):
                with overflowed(pe):
                    pe.sem_inc(s_ohused, 2)

                    def products(k, c, start, stop):
                        n = k * EC + c
                        pe.wait_ge(s_oh, n + 1)
                        for i in range(BPE):
                            w = min(CH, N - CH * i)
                            last = nc.tensor.matmul(ps[i][:, 0:w], onehot_src[:, ds((n % 2) * P, P)],
                                                    onehot_dst[:, ds((n % 2) * NPAD + CH * i, w)], start=start, stop=stop)
                        last.then_inc(s_ohused, 1)
                        return last

                    with pe.Fori(0, KT) as k:
                        pe.wait_ge(s_evac, k + 1)
                        products(k, 0, True, False)
                        with pe.Fori(1, EC - 1) as c:
                            products(k, c, False, False)
                        products(k, EC - 1, False, True)

        s_deg, s_degread, s_rdeg, s_rdegout, s_cr = (sem("s_deg"), sem("s_degread"), sem("s_rdeg"), sem("s_rdegout"),
                                                     sem("s_cr"))
        s_ones = sem("s_ones")
        ones = parts[:, 0:P]

        def width(j):
            return TAIL if isinstance(j, int) and j == NF else CH

        with nc.Block() as block:
            @block.vector
            def _(dve):
                nc.vector.memset(ones, 1.0).then_inc(s_ones, 1)
                for j in range(NCH):
                    w = width(j)
                    dve.wait_ge(s_deg, j + 1)
                    if j >= 1:
                        dve.wait_ge(s_rdegout, 16 * j)
                    nc.vector.tensor_scalar(scratch[:, 0:w], ps[j % 2][:, 0:w], 1.0, None, ALU.max).then_inc(s_degread, 1)
                    dve.wait_ge(s_degread, j + 1)
                    if j == NF:
                        nc.vector.reciprocal(rdeg_tail[:, :], scratch[:, 0:w])
                    else:
                        nc.vector.reciprocal(rdeg[:, :], scratch[:, 0:w]).then_inc(s_rdeg, 1)

            @block.tensor
            def _(pe):
                pe.wait_ge(s_ones, 1)
                for j in range(NCH):
                    w = width(j)
                    if j >= 2:
                        pe.wait_ge(s_degread, j - 1)
                    for k in range(KT):
                        last = nc.tensor.matmul(ps[j % 2][:, 0:w], ones, adj[:, k * N + j * CH:k * N + j * CH + w],
                                                start=(k == 0), stop=(k == KT - 1))
                    last.then_inc(s_deg, 1)

            @block.sync
            def _(sp):
                for j in range(NF):
                    sp.wait_ge(s_rdeg, j + 1)
                    sp.dma_start(rdeg_dram[j], rdeg[:, :]).then_inc(s_rdegout, 16)
                sp.wait_ge(s_rdegout, 16 * NF)

        def layernorm(nc, link, sqrt_ready, root_ready, act_n, eng, xt, xc, sq, a, p):
            sums, mean, var, root, inv, tmp = (stat[0:p, i, 0:a] for i in range(6))

            def over_d(t):
                return t.rearrange("p (a o) -> p a o", o=1).broadcast_to([p, a, D])

            link(nc.vector.tensor_reduce(sums, xt, AX.X, ALU.add))
            link(nc.vector.tensor_scalar(mean, sums, 1.0 / D, None, ALU.mult))
            link(nc.vector.tensor_tensor(xc, xt, over_d(mean), ALU.subtract))
            link(nc.vector.tensor_tensor(sq, xc, xc, ALU.mult))
            link(nc.vector.tensor_reduce(sums, sq, AX.X, ALU.add))
            nc.vector.tensor_scalar(var, sums, 1.0 / D, EPS, ALU.mult, ALU.add).then_inc(sqrt_ready, 1)
            eng.wait_ge(sqrt_ready, act_n)
            eng.wait_ge(root_ready, act_n)
            link(nc.vector.reciprocal(inv, root))
            link(nc.vector.tensor_tensor(tmp, var, inv, ALU.mult))
            link(nc.vector.tensor_tensor(root, root, tmp, ALU.add))
            link(nc.vector.tensor_scalar(root, root, 0.5, None, ALU.mult))
            link(nc.vector.reciprocal(inv, root))
            link(nc.vector.tensor_tensor(xc, xc, over_d(inv), ALU.mult))

        def parity(t):
            if isinstance(t, int):
                return t % 2
            assert t.out_of_modulus % 2 == 0
            return t.guaranteed_mod_val % 2

        def part(t, k, h):
            return ds(parity(t) * PW + k * 2 * D + h * D, D)

        def parts4(t, j, h, a, p):
            v = parts[0:p, ds(parity(t) * PW + j * TPC * 2 * D, a * 2 * D)].rearrange("p (a h d) -> p a h d", a=a, h=2)
            return v[:, :, h, :]

        def tiled(t, a, p):
            return t[0:p, 0:a * D].rearrange("p (a d) -> p a d", a=a)

        s_xin, s_xused, s_var, s_root, s_cl = sem("s_xin"), sem("s_xused"), sem("s_var"), sem("s_root"), sem("s_cl")
        s_hi0 = sem("s_hi0")
        s_zero = sem("s_zero")
        x_buf = hidden[:, 0, :]
        xc_buf = hidden[:, 1, :]
        sq_buf = scratch
        with nc.Block() as block:
            @block.sync
            def _(sp):
                for j in range(NCH):
                    a, p = (1, TAIL) if j == NF else (TPC, P)
                    if j >= 1:
                        sp.wait_ge(s_xused, j)
                    sp.dma_start(tiled(x_buf, a, p) if j < NF else x_buf[0:p, 0:D], node_rows(x, j)).then_inc(s_xin, 16)

            @block.scalar
            def _(act):
                for j in range(NCH):
                    a, p = (1, TAIL) if j == NF else (TPC, P)
                    act.wait_ge(s_var, j + 1)
                    nc.scalar.activation(stat[0:p, 3, 0:a], stat[0:p, 2, 0:a], ACT.Sqrt).then_inc(s_root, 1)

            @block.vector
            def _(dve):
                link = Chain(dve, s_cl)
                link(nc.vector.memset(parts[:, :], 0.0))
                link(nc.vector.memset(state[:, N:KT * P], 0.0))
                for j in range(NCH):
                    a, p = (1, TAIL) if j == NF else (TPC, P)
                    dve.wait_ge(s_xin, 16 * (j + 1))
                    layernorm(nc, link, s_var, s_root, j + 1, dve, tiled(x_buf, a, p), tiled(xc_buf, a, p),
                              tiled(sq_buf, a, p), a, p)
                    link(nc.vector.tensor_scalar(tiled(sq_buf, a, p), tiled(xc_buf, a, p), 0.0, LN_SCALE, ALU.max, ALU.mult))
                    link(nc.vector.tensor_copy(parts4(1, j, 0, a, p), tiled(sq_buf, a, p)))
                    ins = nc.vector.tensor_tensor(parts4(1, j, 1, a, p), tiled(sq_buf, a, p), parts4(1, j, 0, a, p),
                                                  ALU.subtract)
                    link.n += 0
                    ins.then_inc(s_xused, 1)
                    dve.wait_ge(s_xused, j + 1)

        def aggregate(eng, bank, t, j, wait_parts=None, between=None):
            w = width(j)
            for k in range(KT):
                if wait_parts is not None:
                    wait_parts(k)
                for h in range(2):
                    last = nc.tensor.matmul(bank[:, 0:w], parts[:, part(t, k, h)], adj[:, ds(j * CH + k * N, w)],
                                            start=(k == 0 and h == 0), stop=(k == KT - 1 and h == 1))
                if between is not None:
                    between(k)
            return last

        s_g, s_sum, s_y = sem("s_g"), sem("s_sum"), sem("s_y")
        s_xin1, s_x1out, s_var1, s_root1, s_cf = (sem("s_xin1"), sem("s_x1out"), sem("s_var1"), sem("s_root1"),
                                                  sem("s_cf"))
        s_x1, s_ln, s_lnt, s_lntc, s_in, s_st, s_stt, s_hi, s_lo = (
            sem("s_x1"), sem("s_ln"), sem("s_lnt"), sem("s_lntc"), sem("s_in"), sem("s_st"), sem("s_stt"),
            sem("s_hi"), sem("s_lo"))
        x1_buf = diff
        lnt_buf = rdeg
        with nc.Block() as block:
            @block.sync
            def _(sp):
                for j in range(NCH):
                    a, p = (1, TAIL) if j == NF else (TPC, P)
                    wait(sp, s_x1, j)
                    sp.dma_start(tiled(x_buf, a, p) if j < NF else x_buf[0:p, 0:D], node_rows(x, j)).then_inc(s_xin1, 16)
                    sp.wait_ge(s_x1, j + 1)
                    sp.dma_start(node_rows(x1_dram, j), tiled(x1_buf, a, p) if j < NF else x1_buf[0:p, 0:D])\
                        .then_inc(s_x1out, 16)
                sp.wait_ge(s_x1out, 16 * NCH)

            @block.tensor
            def _(pe):
                def product(j):
                    a, p = (1, TAIL) if j == NF else (TPC, P)
                    pe.wait_ge(s_sum, j + 1)
                    wait(pe, s_x1, j)
                    for i in range(a):
                        last = nc.tensor.matmul(ps[2][0:p, i * D:(i + 1) * D], agg[:, i * P:i * P + p], w0t[:, :],
                                                start=True, stop=True)
                    last.then_inc(s_y, 1)

                def normed_to_features(j):
                    a, p = (1, TAIL) if j == NF else (TPC, P)
                    pe.wait_ge(s_ln, j + 1)
                    wait(pe, s_lntc, j)
                    for i in range(a):
                        last = nc.tensor.transpose(ps[3][:, i * P:i * P + p], xc_buf[0:p, i * D:(i + 1) * D],
                                                   ident[0:p, 0:p])
                    last.then_inc(s_lnt, 1)

                def input_product(j):
                    w = width(j)
                    pe.wait_ge(s_lntc, j + 1)
                    wait(pe, s_st, j)
                    nc.tensor.matmul(ps[4][:, 0:w], w_in[:, :], lnt_buf[:, 0:w], start=True, stop=True).then_inc(s_in, 1)

                def state_to_nodes(j):
                    a, p = (1, TAIL) if j == NF else (TPC, P)
                    pe.wait_ge(s_st, j + 1)
                    wait(pe, s_lo, j)
                    for i in range(a):
                        last = nc.tensor.transpose(ps[5][:, i * D:(i + 1) * D],
                                                   state[:, j * CH + i * P:j * CH + (i + 1) * P], ident[:, :])
                    last.then_inc(s_stt, 1)

                for j in range(NCH):
                    def between(k, j=j):
                        if j >= 1 and k == 2:
                            product(j - 1)
                        if j >= 2 and k == 4:
                            normed_to_features(j - 2)
                        if j >= 2 and k == 9:
                            input_product(j - 2)
                        if j >= 2 and k == 16:
                            state_to_nodes(j - 2)
                    if j >= 2:
                        pe.wait_ge(s_sum, j - 1)
                    aggregate(pe, ps[j % 2], 1, j, between=between).then_inc(s_g, 1)
                product(NF)
                for j in (NF - 1, NF):
                    normed_to_features(j)
                    input_product(j)
                    state_to_nodes(j)

            @block.scalar
            def _(act):
                def root(j):
                    a, p = (1, TAIL) if j == NF else (TPC, P)
                    act.wait_ge(s_var1, j + 1)
                    nc.scalar.activation(stat[0:p, 3, 0:a], stat[0:p, 2, 0:a], ACT.Sqrt).then_inc(s_root1, 1)

                def second_input(j):
                    w = width(j)
                    a, p = (1, TAIL) if j == NF else (TPC, P)
                    act.wait_ge(s_lnt, j + 1)
                    wait(act, s_in, j)
                    nc.scalar.activation(lnt_buf[:, 0:w], ps[3][:, 0:w], ACT.Copy).then_inc(s_lntc, 1)
                    act.wait_ge(s_in, j + 1)
                    nc.scalar.activation(state[:, j * CH:j * CH + w], ps[4][:, 0:w], ACT.Tanh,
                                         bias=b_in_col[:, :]).then_inc(s_st, 1)
                    act.wait_ge(s_stt, j + 1)
                    nc.scalar.activation(parts4(0, j, 0, a, p), tiled(ps[5], a, p), ACT.Copy,
                                         scale=scale[0:p, 0:1]).then_inc(s_hi, 1)

                for j in range(NCH):
                    root(j)
                    if j >= 1:
                        second_input(j - 1)
                second_input(NF)

            @block.vector
            def _(dve):
                link = Chain(dve, s_cf)

                def sums(j):
                    w = width(j)
                    dve.wait_ge(s_g, j + 1)
                    wait(dve, s_y, j)
                    nc.vector.tensor_scalar(agg[:, 0:w], ps[j % 2][:, 0:w], 1.0 / LN_SCALE, None, ALU.mult)\
                        .then_inc(s_sum, 1)

                def normed(j):
                    a, p = (1, TAIL) if j == NF else (TPC, P)
                    dve.wait_ge(s_y, j + 1)
                    dve.wait_ge(s_xin1, 16 * (j + 1))
                    wait(dve, s_x1out, 16 * j)
                    link(nc.vector.tensor_tensor(tiled(x1_buf, a, p), tiled(ps[2], a, p), tiled(x_buf, a, p), ALU.add))
                    nc.vector.tensor_tensor(
                        tiled(x1_buf, a, p), tiled(x1_buf, a, p),
                        b0_row[0:p, :].rearrange("p (o d) -> p o d", o=1).broadcast_to([p, a, D]), ALU.add)\
                        .then_inc(s_x1, 1)
                    dve.wait_ge(s_x1, j + 1)
                    wait(dve, s_lnt, j)
                    layernorm(nc, link, s_var1, s_root1, j + 1, dve, tiled(x1_buf, a, p), tiled(xc_buf, a, p),
                              tiled(sq_buf, a, p), a, p)
                    nc.vector.tensor_scalar(tiled(xc_buf, a, p), tiled(xc_buf, a, p), 0.0, None, ALU.max)\
                        .then_inc(s_ln, 1)

                def low_halves(j):
                    a, p = (1, TAIL) if j == NF else (TPC, P)
                    dve.wait_ge(s_hi, j + 1)
                    nc.vector.scalar_tensor_tensor(parts4(0, j, 1, a, p), tiled(ps[5], a, p), scale[0:p, 0:1],
                                                   parts4(0, j, 0, a, p), ALU.mult, ALU.subtract).then_inc(s_lo, 1)

                sums(0)
                for j in range(NCH):
                    normed(j)
                    if j >= 1:
                        low_halves(j - 1)
                    if j < NF:
                        sums(j + 1)
                low_halves(NF)

        (t_parts, t_agg, t_aggs, t_hid, t_gelu, t_out, t_tanh, t_state, t_tr, t_hi, t_rdeg, t_cs,
         t_x1, t_fin, t_store, t_scale) = (
            sem("t_parts"), sem("t_agg"), sem("t_aggs"), sem("t_hid"), sem("t_gelu"),
            sem("t_out"), sem("t_tanh"), sem("t_state"), sem("t_tr"), sem("t_hi"), sem("t_rdeg"), sem("t_cs"),
            sem("t_x1"), sem("t_fin"), sem("t_store"), sem("t_scale"))
        HIDB, OUTB, TRB = (ps[3], ps[4]), ps[5], ps[6]
        LAST = STEPS - 1

        def agg_bank(j):
            return ps[2] if isinstance(j, int) and j == NF else ps[j % 2]

        def shape_of(j):
            return (1, TAIL) if j == NF else (TPC, P)

        def state_cols(j, i=0, n=None):
            return state[:, ds(j * CH + i * P, width(j) if n is None else n)]

        with nc.Block() as block:
            @block.sync
            def _(sp):
                def step(t):
                    for j in range(NF):
                        m = t * NF + j
                        if j >= 1:
                            sp.wait_ge(t_aggs, t * NCH + j)
                        elif not isinstance(t, int):
                            sp.wait_ge(t_aggs, t * NCH - 1)
                        sp.dma_start(rdeg[:, :], rdeg_dram[j]).then_inc(t_rdeg, 16)
                step(0)
                with sp.Fori(1, STEPS) as t:
                    step(t)
                for j in range(NCH):
                    a, p = shape_of(j)
                    n = LAST * NCH + j
                    if j == 0:
                        sp.wait_ge(t_gelu, 2 * STEPS * NCH)
                    else:
                        sp.wait_ge(t_fin, j)
                    sp.dma_start(tiled(scratch, a, p) if j < NF else scratch[0:p, 0:D], node_rows(x1_dram, j)).then_inc(t_x1, 16)
                    sp.wait_ge(t_fin, j + 1)
                    sp.dma_start(node_rows(out, j), tiled(rdeg, a, p) if j < NF else rdeg[0:p, 0:D]).then_inc(t_store, 16)
                sp.wait_ge(t_store, 16 * NCH)

            @block.tensor
            def _(pe):
                def chunk_sum(t, j, wait_parts=None, between=None):
                    n = t * NCH + j
                    if not (isinstance(n, int) and n < 2):
                        wait(pe, t_aggs, n - 1)
                    aggregate(pe, agg_bank(j), t, j, wait_parts, between).then_inc(t_agg, 1)

                def project_up(t, j):
                    n = t * NCH + j
                    w = width(j)
                    wait(pe, t_aggs, n + 1)
                    src_t = agg_tail if j == NF else agg
                    for half in range(2):
                        wait(pe, t_gelu, 2 * n)
                        nc.tensor.matmul(HIDB[half][:, 0:w], w1[:, half * P:(half + 1) * P], src_t[:, 0:w],
                                         start=True, stop=True).then_inc(t_hid, 1)

                def project_down(t, j):
                    n = t * NCH + j
                    w = width(j)
                    wait(pe, t_tanh, n)
                    for half in range(2):
                        wait(pe, t_gelu, 2 * n + 1 + half)
                        last = nc.tensor.matmul(OUTB[:, 0:w], w2[:, half, :], hidden[:, half, 0:w],
                                                start=(half == 0), stop=(half == 1))
                    last.then_inc(t_out, 1)

                def to_nodes(t, j, final=False):
                    n = t * NCH + j
                    a, p = shape_of(j)
                    wait(pe, t_state, n + 1)
                    if final:
                        if j >= 1:
                            wait(pe, t_fin, j)
                        else:
                            wait(pe, t_parts, LAST * NCH)
                    else:
                        wait(pe, t_parts, n)
                    for i in range(a):
                        last = nc.tensor.transpose(TRB[:, i * D:(i + 1) * D], state_cols(j, i, P), ident[:, :])
                    last.then_inc(t_tr, 1)

                def middle(t, final=False):
                    for j in range(1, NCH):
                        def between(k, j=j):
                            if k == 3:
                                project_up(t, j - 1)
                            if k == 11:
                                project_down(t, j - 1)
                            if k == 19 and not final:
                                to_nodes(t, j - 1)
                        chunk_sum(t, j, between=between if j < NF else None)

                def bridge(t):
                    def wait_parts(k):
                        if k == 0:
                            wait(pe, t_parts, t * NCH + NF - 1)
                        if k == (NF - 1) * TPC:
                            wait(pe, t_parts, t * NCH + NF)
                        if k == NF * TPC:
                            wait(pe, t_parts, (t + 1) * NCH)

                    def between(k):
                        if k == 1:
                            project_up(t, NF - 1)
                        if k == 6:
                            project_down(t, NF - 1)
                        if k == 7:
                            project_up(t, NF)
                        if k == 10:
                            to_nodes(t, NF - 1)
                        if k == 15:
                            project_down(t, NF)
                        if k == 19:
                            to_nodes(t, NF)
                    chunk_sum(t + 1, 0, wait_parts, between)

                chunk_sum(0, 0)
                middle(0)
                bridge(0)
                with pe.Fori(0, (LAST - 1) // 2) as pair:
                    for t in (pair * 2 + 1, pair * 2 + 2):
                        middle(t)
                        bridge(t)
                middle(LAST, True)
                for j in (NF - 1, NF):
                    project_up(LAST, j)
                    project_down(LAST, j)
                for j in range(NCH):
                    to_nodes(LAST, j, True)

            @block.scalar
            def _(act):
                def dense(t, j, final=False):
                    n = t * NCH + j
                    w = width(j)
                    for half in range(2):
                        wait(act, t_hid, 2 * n + 1 + half)
                        wait(act, t_out, n)
                        nc.scalar.activation(hidden[:, half, 0:w], HIDB[half][:, 0:w], ACT.Gelu,
                                             bias=b1_col[:, half:half + 1]).then_inc(t_gelu, 1)
                    wait(act, t_out, n + 1)
                    wait(act, t_state, n)
                    nc.scalar.activation(diff[:, 0:w], OUTB[:, 0:w], ACT.Tanh, bias=b2_col[:, :]).then_inc(t_tanh, 1)
                    if not final:
                        a, p = shape_of(j)
                        wait(act, t_tr, n + 1)
                        nc.scalar.activation(parts4(t + 1, j, 0, a, p), tiled(TRB, a, p), ACT.Copy,
                                             scale=step_scale[0:p, 1:2]).then_inc(t_hi, 1)

                for j in range(NCH):
                    dense(0, j)
                with act.Fori(0, (LAST - 1) // 2) as pair:
                    for t in (pair * 2 + 1, pair * 2 + 2):
                        for j in range(NCH):
                            dense(t, j)
                for j in range(NCH):
                    dense(LAST, j, True)

            @block.vector
            def _(dve):
                def scale_out(t, j):
                    n = t * NCH + j
                    w = width(j)
                    wait(dve, t_agg, n + 1)
                    if j < NF:
                        wait(dve, t_rdeg, 16 * (t * NF + j + 1))
                    wait(dve, t_hid, 2 * (n - NF) if j == NF else 2 * n)
                    dst_t, r = (agg_tail, rdeg_tail) if j == NF else (agg, rdeg)
                    nc.vector.scalar_tensor_tensor(dst_t[:, 0:w], agg_bank(j)[:, 0:w], step_scale[:, 0:1], r[:, 0:w],
                                                   ALU.mult, ALU.mult).then_inc(t_aggs, 1)

                def dense(t, j, final):
                    n = t * NCH + j
                    w = width(j)
                    wait(dve, t_tanh, n + 1)
                    nc.vector.scalar_tensor_tensor(diff[:, 0:w], state_cols(j), decay[:, 1:2], diff[:, 0:w],
                                                   ALU.mult, ALU.add).then_inc(t_cs, 1)
                    wait(dve, t_cs, n + 1)
                    nc.vector.scalar_tensor_tensor(state_cols(j), diff[:, 0:w], DT, state_cols(j),
                                                   ALU.mult, ALU.add).then_inc(t_state, 1)
                    a, p = shape_of(j)
                    if not final:
                        wait(dve, t_hi, n + 1)
                        nc.vector.scalar_tensor_tensor(parts4(t + 1, j, 1, a, p), tiled(TRB, a, p),
                                                       step_scale[0:p, 1:2], parts4(t + 1, j, 0, a, p),
                                                       ALU.mult, ALU.subtract).then_inc(t_parts, 1)

                def finish(t, j):
                    a, p = shape_of(j)
                    wait(dve, t_tr, t * NCH + j + 1)
                    wait(dve, t_x1, 16 * (j + 1))
                    if j >= 1:
                        wait(dve, t_store, 16 * j)
                    nc.vector.tensor_tensor(tiled(rdeg, a, p), tiled(scratch, a, p), tiled(TRB, a, p), ALU.add)\
                        .then_inc(t_fin, 1)

                def step(t, final=False):
                    wait(dve, t_aggs, t * NCH)
                    wait(dve, t_parts, t * NCH)
                    nc.vector.tensor_copy(step_scale[:, 0:1], unscale[:, ds(t, 1)])
                    nc.vector.tensor_copy(step_scale[:, 1:2], scale[:, ds(t + 1, 1)]).then_inc(t_scale, 1)
                    wait(dve, t_scale, t + 1)
                    scale_out(t, 0)
                    for j in range(1, NF):
                        dense(t, j - 1, final)
                        scale_out(t, j)
                    scale_out(t, NF)
                    dense(t, NF - 1, final)
                    dense(t, NF, final)

                step(0)
                with dve.Fori(0, (LAST - 1) // 2) as pair:
                    step(pair * 2 + 1)
                    step(pair * 2 + 2)
                step(LAST, True)
                for j in range(NCH):
                    finish(LAST, j)


_INS = ['x', 'src', 'dst', 'L0_gnn_W', 'L0_gnn_b', 'L1_gnn_W_in', 'L1_gnn_b_in', 'L1_gnn_W1', 'L1_gnn_b1', 'L1_gnn_W2',
        'L1_gnn_b2', 'L1_gnn_clearance']


def kernel(**inputs):
    import numpy as _np
    import concourse.bacc as _bacc
    from concourse import mybir as _mybir
    from concourse.bass_utils import run_bass_kernel_spmd as _run

    nc = _bacc.Bacc("TRN2", target_bir_lowering=False, num_devices=1)
    arrays, args = {}, []
    for name in _INS:
        a = _np.ascontiguousarray(inputs[name])
        arrays[f"in_{name}"] = a
        args.append(nc.dram_tensor(f"in_{name}", a.shape, _mybir.dt.from_np(a.dtype), kind="ExternalInput").ap())
    shape = inputs['x'].shape
    args.append(nc.dram_tensor("out_0", shape, _mybir.dt.float32, kind="ExternalOutput").ap())
    graph_layers_kernel(nc, *args)
    r = _run(nc, [arrays], core_ids=[0])
    return r.results[0]["out_0"]
```
